# Optimizing a Trainium2 kernel written in Bass

```python
import numpy as np
import jax
import jax.numpy as jnp

def _softmax(x, axis=-1):
    return jax.nn.softmax(x, axis=axis)

def _gelu(x):
    return jax.nn.gelu(x, approximate=True)

def _silu(x):
    return jax.nn.silu(x)

def _sigmoid(x):
    return jax.nn.sigmoid(x)

def _layernorm(x, axis=-1, eps=1e-05):
    m = jnp.mean(x, axis=axis, keepdims=True)
    v = jnp.var(x, axis=axis, keepdims=True)
    return (x - m) / jnp.sqrt(v + eps)

def _scatter_add(tgt, idx, src, axis=0):
    return tgt.at[idx].add(src)

def _segment_sum(src, seg, n):
    return jax.ops.segment_sum(src, seg, n)
kernel_name = 'mk_gnn_resnorm_d2_gnn_r8_466ef2'

def setup_inputs(seed: int=0):
    np.random.seed(seed)
    _w = jnp.asarray

    def _rec_inputs():
        import jax
        import jax.numpy as jnp
        _gk = jax.random.key(seed)
        x = -0.0002117 + 1 * jax.random.normal(jax.random.fold_in(_gk, 1), (6250, 512), jnp.float32)
        _s = jax.random.randint(jax.random.fold_in(_gk, 2), (50000,), 0, 6250, jnp.int32)
        _d = jax.random.randint(jax.random.fold_in(_gk, 3), (50000,), 0, 6250, jnp.int32)
        _loop = jnp.arange(6250, dtype=jnp.int32)
        src = jnp.concatenate([_s, _d, _loop])
        dst = jnp.concatenate([_d, _s, _loop])
        _o = jnp.argsort(dst, stable=True)
        src = src[_o]
        dst = dst[_o]
        return (x, src, dst)
    x, src, dst = _rec_inputs()

    def _L0_gnn_setup():
        import jax, jax.numpy as jnp
        import numpy as np
        N_NODES = 6250
        key = jax.random.key(seed)
        ks = jax.random.split(key, 5)
        d_in, d_out = (512, 512)
        n_edges = 100000
        x = jax.random.normal(ks[0], (N_NODES, d_in), dtype=jnp.float32)
        edge_index = jax.random.randint(ks[1], (2, n_edges), 0, N_NODES, dtype=jnp.int64)
        s = 1.0 / np.sqrt(d_in)
        W_l = jax.random.uniform(ks[2], (d_out, d_in), dtype=jnp.float32, minval=-s, maxval=s)
        b_l = jax.random.uniform(ks[3], (d_out,), dtype=jnp.float32, minval=-s, maxval=s)
        W_r = jax.random.uniform(ks[4], (d_out, d_in), dtype=jnp.float32, minval=-s, maxval=s)
        return {'x': x, 'edge_index': edge_index, 'W_l': W_l, 'b_l': b_l, 'W_r': W_r}
    _L0_gnn_all = _L0_gnn_setup()
    _L0_gnn_in = {k: v for k, v in _L0_gnn_all.items() if k in ('W_l', 'b_l', 'W_r')}
    del _L0_gnn_all

    def _L1_gnn_setup():
        import jax, jax.numpy as jnp
        import numpy as np
        N_NODES = 1250
        N_EDGES = 20000
        DIM = 512
        LN_EPS = 1e-05
        key = jax.random.key(seed)
        ks = jax.random.split(key, 6)
        scale = 1.0 / np.sqrt(DIM)
        h = jax.random.normal(ks[0], (N_NODES, DIM), dtype=jnp.float32)
        edge_index = jax.random.randint(ks[1], (2, N_EDGES), 0, N_NODES, dtype=jnp.int32)
        W_self = jax.random.normal(ks[2], (DIM, DIM), dtype=jnp.float32) * scale
        b_self = jnp.zeros((DIM,), dtype=jnp.float32)
        W_neigh = jax.random.normal(ks[3], (DIM, DIM), dtype=jnp.float32) * scale
        b_neigh = jnp.zeros((DIM,), dtype=jnp.float32)
        ln_gamma = jnp.ones((DIM,), dtype=jnp.float32)
        ln_beta = jnp.zeros((DIM,), dtype=jnp.float32)
        return {'h': h, 'edge_index': edge_index, 'W_self': W_self, 'b_self': b_self, 'W_neigh': W_neigh, 'b_neigh': b_neigh, 'ln_gamma': ln_gamma, 'ln_beta': ln_beta}
    _L1_gnn_all = _L1_gnn_setup()
    _L1_gnn_in = {k: v for k, v in _L1_gnn_all.items() if k in ('W_self', 'b_self', 'W_neigh', 'b_neigh', 'ln_gamma', 'ln_beta')}
    del _L1_gnn_all
    return {'x': x, 'src': src, 'dst': dst, 'L0_gnn_W_l': _L0_gnn_in['W_l'], 'L0_gnn_b_l': _L0_gnn_in['b_l'], 'L0_gnn_W_r': _L0_gnn_in['W_r'], 'L1_gnn_W_self': _L1_gnn_in['W_self'], 'L1_gnn_b_self': _L1_gnn_in['b_self'], 'L1_gnn_W_neigh': _L1_gnn_in['W_neigh'], 'L1_gnn_b_neigh': _L1_gnn_in['b_neigh'], 'L1_gnn_ln_gamma': _L1_gnn_in['ln_gamma'], 'L1_gnn_ln_beta': _L1_gnn_in['ln_beta']}

def reference(x, src, dst, L0_gnn_W_l, L0_gnn_b_l, L0_gnn_W_r, L1_gnn_W_self, L1_gnn_b_self, L1_gnn_W_neigh, L1_gnn_b_neigh, L1_gnn_ln_gamma, L1_gnn_ln_beta):
    import jax
    import jax.numpy as jnp

    def _L0_gnn_ref(x, edge_index, W_l, b_l, W_r):
        import jax, jax.numpy as jnp
        import numpy as np
        N_NODES = 6250
        x_l = x @ W_l.T + b_l
        src, dst = (edge_index[0], edge_index[1])
        agg = jax.ops.segment_sum(x_l[src], dst, num_segments=N_NODES)
        deg = jax.ops.segment_sum(jnp.ones_like(src, dtype=x.dtype), dst, num_segments=N_NODES)
        out_l = agg / jnp.maximum(deg, 1.0)[:, None]
        out_r = x @ W_r.T
        return out_l + out_r

    def _L1_gnn_ref(h, edge_index, W_self, b_self, W_neigh, b_neigh, ln_gamma, ln_beta):
        import jax, jax.numpy as jnp
        import numpy as np
        N_NODES = 1250
        N_EDGES = 20000
        DIM = 512
        LN_EPS = 1e-05
        n = h.shape[0]
        src = edge_index[0]
        dst = edge_index[1]
        msg = h[dst] @ W_neigh.T + b_neigh
        neigh = jax.ops.segment_sum(msg, src, num_segments=n)
        deg = jax.ops.segment_sum(jnp.ones(src.shape, h.dtype), src, num_segments=n)
        deg = jnp.maximum(deg, 1.0)
        neigh = neigh / deg[:, None]
        out = jax.nn.relu(h @ W_self.T + b_self + neigh)
        x = h + out
        mean = jnp.mean(x, axis=-1, keepdims=True)
        var = jnp.mean(jnp.square(x - mean), axis=-1, keepdims=True)
        return (x - mean) * jax.lax.rsqrt(var + LN_EPS) * ln_gamma + ln_beta
    edge_index = jnp.stack([src, dst])
    x = _layernorm(x + _L0_gnn_ref(x, edge_index, L0_gnn_W_l, L0_gnn_b_l, L0_gnn_W_r), axis=-1)
    x = _layernorm(x + _L1_gnn_ref(x, edge_index, L1_gnn_W_self, L1_gnn_b_self, L1_gnn_W_neigh, L1_gnn_b_neigh, L1_gnn_ln_gamma, L1_gnn_ln_beta), axis=-1)
    return x

_drawn_inputs = setup_inputs


def setup_inputs(seed=0):
    import zlib

    import numpy as np

    out = dict(_drawn_inputs(seed))
    spreads = {'L1_gnn_b_self': (0.0, 0.268),
     'L1_gnn_b_neigh': (0.0, 0.27),
     'L1_gnn_ln_gamma': (1.0, 0.2),
     'L1_gnn_ln_beta': (0.0, 0.1)}
    factors = {}
    for name, (base, spread) in spreads.items():
        noise = np.random.default_rng([zlib.crc32(name.encode()), seed]).standard_normal(out[name].shape)
        drawn = base * np.exp(spread * noise) if base else spread * noise
        out[name] = jnp.asarray(drawn.astype(out[name].dtype))
    for name, factor in factors.items():
        out[name] = (out[name] * factor).astype(out[name].dtype)
    return out
```

```python
import concourse.bass as bass
from concourse import mybir
from contextlib import ExitStack

P = 128


def gnn_two_layers(nc, x, src, dst, w_l_t, b_l, w_r_t, w_self_t, b_self, w_neigh_t, b_neigh, gamma, beta, out):
    f32, f16, i32 = mybir.dt.float32, mybir.dt.float16, mybir.dt.int32
    ALU, ACT, AX = mybir.AluOpType, mybir.ActivationFunctionType, mybir.AxisListType
    ds = bass.ds

    N, D = x.shape
    E = src.shape[0]
    EP = 125
    EC = E // EP
    assert EP * EC == E
    T = -(-N // P)
    LAST = N - (T - 1) * P
    U = 16
    H = U // 2
    C = -(-(-(-E // P) + T) // U) * U
    ITER = C // U
    KC = D // P
    CH = C // 2
    assert CH <= 512
    EPS = 1e-5
    GB = 8
    SB = 4

    ctx = ExitStack()
    with ctx:
        def sb(name, shape, dt):
            return ctx.enter_context(nc.sbuf_tensor(name, shape, dt))

        def sem(name):
            return ctx.enter_context(nc.semaphore(name))

        tri = sb("tri", [P, P], f32)
        ones = sb("ones", [P, P], f32)
        ident = sb("ident", [P, P], f32)
        iota_node = sb("iota_node", [P, P], f16)
        iota_chunk = sb("iota_chunk", [P, C], f16)
        iota_bin = sb("iota_bin", [P, T], f32)
        edges = sb("edges", [EP, 2, EC], i32)
        scratch = sb("scratch", [P, 6, EC], f32)
        inta = scratch[0:EP, 0, :].bitcast(i32)
        intb = scratch[0:EP, 1, :].bitcast(i32)
        binf = sb("binf", [EP, EC], f16)
        val1 = scratch[0:EP, 2, :]
        val2 = scratch[0:EP, 3, :]
        mask = sb("mask", [EP, EC], f16)
        run = scratch[0:EP, 4, :]
        pos = scratch[0:EP, 5, :]
        totals = sb("totals", [EP, T], f32)
        nch = sb("nch", [P, T], f32)
        nchi = sb("nchi", [P, T], i32)
        cend = sb("cend", [P, T], f32)
        cstart = sb("cstart", [P, T], f32)
        base = sb("base", [P, T], f32)
        cs_col = sb("cs_col", [T, 1], f32)
        put1 = sb("put1", [EP, 2, P], f16)
        put2 = sb("put2", [EP, 2, P], f16)
        where = sb("where", [EP, 2, C], f16)
        g_idx = [sb(f"g_idx{l}", [P, C], i32) for l in range(2)]
        g_loc = [sb(f"g_loc{l}", [P, C], f32) for l in range(2)]
        g_tile = [sb(f"g_tile{l}", [1, C], i32) for l in range(2)]
        idx_ring = sb("idx_ring", [P, U], i32)
        rows = sb("rows", [P, GB, D], f32)
        hi, lo = run, pos
        past = rows[0:T, 0:2, :].rearrange("p b d -> p (b d)")[:, 0:C]
        v2i = rows[:, 2:4, :].bitcast(i32).rearrange("p b d -> p (b d)")[:, 0:C]
        v2h = rows[:, 4:6, :].bitcast(i32).rearrange("p b d -> p (b d)")[:, 0:C]
        onehot = sb("onehot", [P, SB, P], f32)
        acc = sb("acc", [P, T, D + 1], f32)
        rdeg = sb("rdeg", [P, T], f32)
        has = sb("has", [P, T], f32)
        w_a = sb("w_a", [P, KC, D], f32)
        w_b = sb("w_b", [P, KC, D], f32)
        vec = sb("vec", [P, 5, D], f32)
        own = rows[:, 0:2, :]
        mean_nb = scratch[:, 0, 0:D]
        t_nb = scratch[:, 1, 0:D]
        t_own = scratch[:, 2, 0:D]
        r = scratch[:, 3, 0:D]
        y = scratch[:, 4, 0:D]
        res = rows[:, 2:4, :]
        st = sb("st", [P, 6], f32)
        mv = sb("mv", [P, 2], f32)
        sd = sb("sd", [P, 1], f32)
        rs = sb("rs", [P, 1], f32)
        eps = sb("eps", [P, 1], f32)
        ps = ctx.enter_context(nc.psum_tensor("ps", [P, 8, 512], f32))

        h_dram = nc.dram_tensor("h_scratch", [T * P, D], f32, kind="Internal").ap()

        s_edges = sem("s_edges")
        s_vec = sem("s_vec")
        s_iota = sem("s_iota")
        s_sel = sem("s_sel")
        s_const = sem("s_const")
        s_w = sem("s_w")
        v = sem("v")
        s_tot = sem("s_tot")
        s_cnt = sem("s_cnt")
        s_cs = sem("s_cs")
        s_cscol = sem("s_cscol")
        s_cscp = sem("s_cscp")
        s_past = sem("s_past")
        s_tile = sem("s_tile")
        s_put = sem("s_put")
        s_placed = sem("s_placed")
        s_list = sem("s_list")
        s_idx = sem("s_idx")
        s_row = [sem(f"s_row{k}") for k in range(GB)]
        s_hot = sem("s_hot")
        s_mm = sem("s_mm")
        s_acc = sem("s_acc")
        s_deg = sem("s_deg")
        s_own = [sem(f"s_own{k}") for k in range(2)]
        s_mean = sem("s_mean")
        s_tr = sem("s_tr")
        s_tc = sem("s_tc")
        s_proj = sem("s_proj")
        s_var = sem("s_var")
        s_sd = sem("s_sd")
        s_res = sem("s_res")
        s_st = [sem(f"s_st{k}") for k in range(2)]

        block = ctx.enter_context(nc.Block())
        NV = {0: 1, 1: 2}

        @block.sync
        def _(sp):
            sp.dma_start(edges[:, 0, :], src.rearrange("(p c) -> p c", p=EP)).then_inc(s_edges, 16)
            sp.dma_start(edges[:, 1, :], dst.rearrange("(p c) -> p c", p=EP)).then_inc(s_edges, 16)
            for n, a in enumerate((b_l, b_self, b_neigh, gamma, beta)):
                sp.dma_start(vec[:, n, :], a.rearrange("(o d) -> o d", o=1).to_broadcast([P, D])).then_inc(s_vec, 16)
            for layer in range(2):
                wa, wb = ((w_l_t, w_r_t), (w_neigh_t, w_self_t))[layer]
                if layer:
                    sp.wait_ge(s_proj, T)
                sp.dma_start(w_a[:], wa.rearrange("(k p) n -> p k n", p=P)).then_inc(s_w, 16)
                sp.dma_start(w_b[:], wb.rearrange("(k p) n -> p k n", p=P)).then_inc(s_w, 16)
                source = (x, h_dram)[layer]
                target = (h_dram, out)[layer]
                done = layer * T

                def load(t, k, n=P):
                    sp.dma_start(own[0:n, k, :], source[ds(t * P, n), :] if not isinstance(t, int)
                                 else source[t * P:t * P + n, :]).then_inc(s_own[k], 16)

                def store(t, k, n=P):
                    sp.dma_start(target[ds(t * P, n), :] if not isinstance(t, int)
                                 else target[t * P:t * P + n, :], res[0:n, k, :]).then_inc(s_st[k], 16)

                if layer:
                    sp.wait_ge(s_st[0], 16 * ((T + 1) // 2))
                    sp.wait_ge(s_st[1], 16 * (T // 2))
                sp.wait_ge(s_mm, (layer + 1) * C)
                load(0, 0)
                load(1, 1)
                with sp.Fori(0, (T - 1) // 2 - 1) as i:
                    for k in range(2):
                        sp.wait_ge(s_res, done + 2 * i + k + 1)
                        store(2 * i + k, k)
                        load(2 * i + k + 2, k)
                for t in range(T - 3, T):
                    sp.wait_ge(s_res, done + t + 1)
                    last_out = LAST if (layer == 1 and t == T - 1) else P
                    store(t, t % 2, last_out)
                    if t == T - 3:
                        load(T - 1, 0, P if layer else LAST)
            sp.wait_ge(s_st[0], 2 * 16 * ((T + 1) // 2))
            sp.wait_ge(s_st[1], 2 * 16 * (T // 2))

        @block.gpsimd
        def _(pool):
            nc.gpsimd.iota(iota_node[:], pattern=[[1, P]], base=0, channel_multiplier=0,
                           allow_small_or_imprecise_dtypes=True).then_inc(s_iota, 1)
            nc.gpsimd.iota(iota_chunk[:], pattern=[[1, C]], base=0, channel_multiplier=0,
                           allow_small_or_imprecise_dtypes=True).then_inc(s_iota, 1)
            nc.gpsimd.iota(iota_bin[:], pattern=[[1, T]], base=0, channel_multiplier=0,
                           allow_small_or_imprecise_dtypes=True).then_inc(s_iota, 1)
            nc.gpsimd.memset(tri[:], 1.0).then_inc(s_sel, 1)
            nc.gpsimd.memset(ident[:], 0.0).then_inc(s_sel, 1)
            nc.gpsimd.memset(ones[:], 1.0).then_inc(s_const, 1)
            nc.gpsimd.memset(eps[:], EPS).then_inc(s_const, 1)
            pool.wait_ge(s_sel, 2)
            nc.gpsimd.affine_select(out=tri[:], in_=tri[:], compare_op=ALU.is_gt, fill=0.0, base=0,
                                    pattern=[[1, P]], channel_multiplier=-1).then_inc(s_const, 1)
            nc.gpsimd.affine_select(out=ident[:], in_=ident[:], compare_op=ALU.not_equal, fill=1.0, base=0,
                                    pattern=[[1, P]], channel_multiplier=-1).then_inc(s_const, 1)

            for layer in range(2):
                table = (x, h_dram)[layer]
                c0, rounds = layer * C, layer * C // GB
                if layer:
                    pool.wait_ge(s_st[0], 16 * ((T + 1) // 2))
                    pool.wait_ge(s_st[1], 16 * (T // 2))

                def gathers(i, first=False):
                    for k in range(U):
                        if k % H == 0:
                            pool.wait_ge(s_idx, layer * 2 * ITER + 2 * i + k // H + 1)
                        if not (first and k < GB):
                            used = c0 + U * i + k - GB + 1
                            if not isinstance(used, int):
                                used = pool.to_reg(used)
                            pool.wait_ge(s_sel, 2)
                            pool.wait_ge(s_mm, used)
                        nc.gpsimd.indirect_dma_start(
                            out=rows[:, k % GB, :], out_offset=None, in_=table[:, :],
                            in_offset=bass.IndirectOffsetOnAxis(ap=idx_ring[:, k:k + 1], axis=0),
                        ).then_inc(s_row[k % GB], 16)

                gathers(0, first=(layer == 0))
                with pool.Fori(1, ITER) as i:
                    gathers(i)

        @block.vector
        def _(dve):
            steps = [0]

            def link(ins):
                steps[0] += 1
                ins.then_inc(v, 1)
                dve.wait_ge(v, steps[0])

            def loop(n, per, body, start=0):
                begun = steps[0]
                with dve.Fori(start, n) as i:
                    steps[0] = begun + (i - start) * per
                    body(i)
                steps[0] = begun + (n - start) * per

            V = nc.vector
            dve.wait_ge(s_edges, 32)
            dve.wait_ge(s_iota, 3)
            for layer in range(2):
                key, other = edges[:, 1 - layer, :], edges[:, layer, :]
                if layer:
                    dve.wait_ge(s_tile, 1)
                link(V.tensor_scalar(inta, key, 7, None, ALU.arith_shift_right))
                link(V.tensor_copy(binf[:], inta))
                link(V.tensor_scalar(inta, other, 3, None, ALU.arith_shift_right))
                link(V.tensor_copy(val1, inta))
                link(V.tensor_scalar(inta, other, 7, 8, ALU.bitwise_and, ALU.logical_shift_left))
                link(V.tensor_scalar(intb, key, 127, None, ALU.bitwise_and))
                link(V.scalar_tensor_tensor(val2, inta, 1.0, intb, ALU.add, ALU.add))

                def count(b):
                    link(V.tensor_scalar(mask[:], binf[:], iota_bin[0:EP, ds(b, 1)], 0.0, ALU.is_equal, ALU.add,
                                         accum_out=totals[:, ds(b, 1)]))
                loop(T, 1, count)
                V.memset(pos, 0.0).then_inc(s_tot, 1)
                dve.wait_ge(s_cnt, layer + 1)
                link(V.tensor_scalar(nchi[:], ps[:, 0, 0:T], float(P - 1), None, ALU.add))
                link(V.tensor_scalar(nchi[:], nchi[:], 7, None, ALU.arith_shift_right))
                link(V.tensor_copy(nch[:], nchi[:]))
                link(V.tensor_tensor_scan(cend[:], nch[:], nch[:], 0.0, ALU.add, ALU.bypass))
                link(V.tensor_tensor(cstart[:], cend[:], nch[:], ALU.subtract))
                link(V.tensor_scalar(base[:], cstart[:], float(P), -1.0, ALU.mult, ALU.add))
                V.tensor_tensor(base[:], base[:], ps[:, 0, 64:64 + T], ALU.add).then_inc(s_cs, 1)
                dve.wait_ge(s_cs, layer + 1)

                def place(b):
                    link(V.tensor_scalar(mask[:], binf[:], iota_bin[0:EP, ds(b, 1)], None, ALU.is_equal))
                    link(V.tensor_tensor_scan(run, mask[:], mask[:], base[0:EP, ds(b, 1)], ALU.add, ALU.bypass))
                    link(V.tensor_tensor(run, run, mask[:], ALU.mult))
                    link(V.tensor_tensor(pos, pos, run, ALU.add))
                loop(T, 4, place)
                link(V.tensor_copy(inta, pos))
                link(V.tensor_scalar(intb, inta, 7, None, ALU.arith_shift_right))
                link(V.tensor_copy(hi, intb))
                link(V.tensor_scalar(intb, inta, 127, None, ALU.bitwise_and))
                link(V.tensor_copy(lo, intb))

                dve.wait_ge(s_cscol, layer + 1)
                V.tensor_copy(cs_col[:], ps[0:T, 0, 128:129]).then_inc(s_cscp, 1)
                dve.wait_ge(s_cscp, layer + 1)
                V.tensor_scalar(past, iota_chunk[0:T, :], cs_col[:, 0:1], None, ALU.is_ge).then_inc(s_past, 1)
                dve.wait_ge(s_past, layer + 1)
                dve.wait_ge(s_tile, layer + 1)
                link(V.tensor_scalar(g_tile[layer].rearrange("p (h c) -> p h c", h=2), ps[0:1, 0:2, 0:CH], -1.0, None, ALU.add))

                g0 = layer * EC

                def puts(c, first=False):
                    for k in range(2):
                        if not first:
                            dve.wait_ge(s_placed, g0 + 2 * c + k - 1)
                        V.tensor_scalar(put1[:, k, :], iota_node[0:EP, :], lo[:, ds(2 * c + k, 1)],
                                        val1[:, ds(2 * c + k, 1)], ALU.is_equal, ALU.mult)
                        V.tensor_scalar(put2[:, k, :], iota_node[0:EP, :], lo[:, ds(2 * c + k, 1)],
                                        val2[:, ds(2 * c + k, 1)], ALU.is_equal, ALU.mult)
                        V.tensor_scalar(where[:, k, :], iota_chunk[0:EP, :], hi[:, ds(2 * c + k, 1)], None,
                                        ALU.is_equal).then_inc(s_put, 1)
                puts(0, first=(layer == 0))
                with dve.Fori(1, EC // 2) as c:
                    puts(c)
                dve.wait_ge(s_placed, g0 + EC)
                halves = "p (h c) -> p h c"
                link(V.tensor_copy(v2i.rearrange(halves, h=2), ps[:, 2:4, 0:CH]))
                link(V.tensor_scalar(v2h, v2i, 8, None, ALU.arith_shift_right))
                link(V.scalar_tensor_tensor(g_idx[layer][:].rearrange(halves, h=2), ps[:, 0:2, 0:CH], 8.0,
                                            v2h.rearrange(halves, h=2), ALU.mult, ALU.add))
                link(V.tensor_scalar(v2h, v2i, 255, None, ALU.bitwise_and))
                V.tensor_scalar(g_loc[layer][:], v2h, -1.0, None, ALU.add).then_inc(s_list, 1)
                dve.wait_ge(s_list, layer + 1)

            for layer in range(2):
                c0 = layer * C
                link(V.memset(acc[:], 0.0))

                def hand_over(i, half):
                    V.tensor_copy(idx_ring[:, half * H:half * H + H],
                                  g_idx[layer][:, ds(i * U + half * H, H)]).then_inc(s_idx, 1)

                def hot(i, k, first=False):
                    if not (first and k < SB):
                        dve.wait_ge(s_mm, c0 + U * i + k - SB + 1)
                    V.tensor_scalar(onehot[:, k % SB, :], iota_node[:], g_loc[layer][:, ds(U * i + k, 1)], None,
                                    ALU.is_equal).then_inc(s_hot, 1)

                def add(i, k, first=False):
                    tile = dve.value_load(g_tile[layer][0:1, ds(U * i + k, 1)], min_val=0, max_val=T - 1)
                    if not (first and k == 0):
                        dve.wait_ge(s_acc, c0 + U * i + k)
                    dve.wait_ge(s_mm, c0 + U * i + k + 1)
                    part = ps[:, 4 + 2 * (k % 2):6 + 2 * (k % 2), :].rearrange("p b c -> p (b c)")[:, 0:D + 1]
                    V.tensor_tensor(acc[:, ds(tile, 1), :].rearrange("p o d -> p (o d)"),
                                    acc[:, ds(tile, 1), :].rearrange("p o d -> p (o d)"), part,
                                    ALU.add).then_inc(s_acc, 1)

                def chunks(i, first=False):
                    for k in range(U):
                        if k == 0 or k == H:
                            half = k // H
                            if not first:
                                dve.wait_ge(s_mm, c0 + U * i + k - H)
                            hand_over(i, half)
                        hot(i, k, first=first and layer == 0)
                        if k >= 1:
                            add(i, k - 1, first=first and layer == 0)
                    add(i, U - 1, first=False)
                chunks(0, first=True)
                with dve.Fori(1, ITER) as i:
                    chunks(i)
                dve.wait_ge(s_acc, c0 + C)
                link(V.tensor_scalar(rdeg[:], acc[:, :, D], 1.0, None, ALU.max))
                link(V.tensor_scalar(has[:], acc[:, :, D], 1.0, None, ALU.min))
                V.reciprocal(rdeg[:], rdeg[:]).then_inc(s_deg, 1)
                if not layer:
                    dve.wait_ge(s_vec, 16 * 5)

                begun = steps[0]
                nvar = layer * T
                per_var = layer + 1
                per = 4 if layer == 0 else 12

                def norm_stats(dest, n):
                    V.bn_stats(st[:], dest).then_inc(v, 1)
                    steps[0] += 1
                    now = steps[0] if isinstance(steps[0], int) else dve.to_reg(steps[0])
                    dve.wait_ge(s_edges, 32)
                    dve.wait_ge(v, now)
                    V.bn_aggr(mv[:], st[:]).then_inc(s_var, 1)
                    dve.wait_ge(s_var, n + 1)
                    dve.wait_ge(s_sd, n + 1)
                    link(V.reciprocal(rs[:], sd[:]))

                def tile(t, k):
                    g = layer * T + t
                    dve.wait_ge(s_proj, g + 1)
                    part = ps[:, 4 + 2 * k, :]
                    if layer == 0:
                        link(V.scalar_tensor_tensor(r, vec[:, 0, :], has[:, ds(t, 1)], part, ALU.mult, ALU.add))
                        link(V.tensor_tensor(r, r, own[:, k, :], ALU.add))
                        norm_stats(r, t)
                        wait_free(t)
                        V.tensor_scalar(res[:, k, :], r, mv[:, 0:1], rs[:, 0:1], ALU.subtract,
                                        ALU.mult).then_inc(s_res, 1)
                        dve.wait_ge(s_res, g + 1)
                    else:
                        link(V.scalar_tensor_tensor(r, vec[:, 2, :], has[:, ds(t, 1)], part, ALU.mult, ALU.add))
                        link(V.tensor_tensor(r, r, vec[:, 1, :], ALU.add))
                        link(V.scalar_tensor_tensor(r, r, 0.0, own[:, k, :], ALU.max, ALU.add))
                        norm_stats(r, nvar + 2 * t)
                        link(V.tensor_scalar(y, r, mv[:, 0:1], rs[:, 0:1], ALU.subtract, ALU.mult))
                        link(V.tensor_tensor(y, y, vec[:, 3, :], ALU.mult))
                        link(V.tensor_tensor(y, y, vec[:, 4, :], ALU.add))
                        link(V.tensor_tensor(y, y, own[:, k, :], ALU.add))
                        norm_stats(y, nvar + 2 * t + 1)
                        wait_free(t)
                        V.tensor_scalar(res[:, k, :], y, mv[:, 0:1], rs[:, 0:1], ALU.subtract,
                                        ALU.mult).then_inc(s_res, 1)
                        dve.wait_ge(s_res, g + 1)

                per = 4 if layer == 0 else 11

                def wait_free(t):
                    pass

                def pair(i, first=False):
                    for k in range(2):
                        if not first:
                            dve.wait_ge(s_st[k], 16 * (layer * ((T + 1 - k) // 2) + i))
                        tile(2 * i + k, k)

                pair(0, first=True)
                assert steps[0] == begun + 2 * per, steps[0] - begun
                begun = steps[0]
                with dve.Fori(1, T // 2) as i:
                    steps[0] = begun + (i - 1) * 2 * per
                    pair(i)
                steps[0] = begun + (T // 2 - 1) * 2 * per
                dve.wait_ge(s_st[0], 16 * (layer * ((T + 1) // 2) + T // 2))
                tile(T - 1, 0)

        @block.tensor
        def _(pe):
            pe.wait_ge(s_const, 4)
            for layer in range(2):
                g0 = layer * EC
                pe.wait_ge(s_tot, layer + 1)
                if layer:
                    pe.wait_ge(s_list, 1)
                nc.tensor.matmul(ps[:, 0, 0:T], ones[0:EP, :], totals[:], start=True, stop=True)
                nc.tensor.matmul(ps[:, 0, 64:64 + T], tri[0:EP, :], totals[:], start=True, stop=True).then_inc(s_cnt, 1)
                pe.wait_ge(s_cs, layer + 1)
                nc.tensor.matmul(ps[0:T, 0, 128:129], cstart[0:1, :], ones[0:1, 0:1], start=True,
                                 stop=True).then_inc(s_cscol, 1)
                pe.wait_ge(s_past, layer + 1)
                for b in range(2):
                    last = nc.tensor.matmul(ps[0:1, b, 0:CH], ones[0:T, 0:1], past[:, b * CH:(b + 1) * CH],
                                            start=True, stop=True)
                last.then_inc(s_tile, 1)

                def place(c, k, start=False, stop=False):
                    pe.wait_ge(s_put, g0 + 2 * c + k + 1)
                    for n, put in enumerate((put1, put2)):
                        for b in range(2):
                            last = nc.tensor.matmul(ps[:, 2 * n + b, 0:CH], put[:, k, :],
                                                    where[:, k, b * CH:(b + 1) * CH], start=start, stop=stop,
                                                    skip_group_check=True)
                    last.then_inc(s_placed, 1)
                place(0, 0, start=True)
                place(0, 1)
                with pe.Fori(1, EC // 2 - 1) as c:
                    place(c, 0)
                    place(c, 1)
                place(EC // 2 - 1, 0)
                place(EC // 2 - 1, 1, stop=True)

            for layer in range(2):
                c0 = layer * C

                def sums(i, first=False):
                    for k in range(U):
                        n = c0 + U * i + k
                        pe.wait_ge(s_hot, n + 1)
                        pe.wait_ge(s_row[k % GB], 16 * (c0 // GB + (U // GB) * i + k // GB + 1))
                        if not (first and k < 2):
                            pe.wait_ge(s_acc, n - 1)
                        nc.tensor.matmul(ps[:, 4 + 2 * (k % 2), :], onehot[:, k % SB, :], rows[:, k % GB, :],
                                         start=True, stop=True)
                        nc.tensor.matmul(ps[:, 5 + 2 * (k % 2), 0:1], onehot[:, k % SB, :], ones[:, 0:1],
                                         start=True, stop=True).then_inc(s_mm, 1)
                sums(0, first=True)
                with pe.Fori(1, ITER) as i:
                    sums(i)

                pe.wait_ge(s_acc, c0 + C)
                pe.wait_ge(s_w, 32 * (layer + 1))

                def tile(t, k, first=False):
                    g = layer * T + t
                    pe.wait_ge(s_mean, g + 1)
                    for j in range(KC):
                        nc.tensor.transpose(ps[:, 0, j * P:(j + 1) * P], mean_nb[:, j * P:(j + 1) * P], ident[:])
                    half = (t - k) // 2 if isinstance(t, int) else None
                    pe.wait_ge(s_own[k], 16 * (layer * ((T + 1 - k) // 2) + tile_round(t, k) + 1))
                    for j in range(KC):
                        last = nc.tensor.transpose(ps[:, 1, j * P:(j + 1) * P], own[:, k, j * P:(j + 1) * P], ident[:])
                    last.then_inc(s_tr, 1)
                    pe.wait_ge(s_tc, g + 1)
                    if not first:
                        pe.wait_ge(s_res, g - 1)
                    for n, (lhs, w) in enumerate(((t_nb, w_a), (t_own, w_b))):
                        for j in range(KC):
                            last = nc.tensor.matmul(ps[:, 4 + 2 * k, :], lhs[:, j * P:(j + 1) * P], w[:, j, :],
                                                    start=(n == 0 and j == 0), stop=(n == 1 and j == KC - 1))
                    last.then_inc(s_proj, 1)

                def tile_round(t, k):
                    return rnd[0]

                rnd = [0]
                tile(0, 0, first=(layer == 0))
                tile(1, 1, first=(layer == 0))
                with pe.Fori(1, T // 2) as i:
                    rnd[0] = i
                    tile(2 * i, 0)
                    tile(2 * i + 1, 1)
                rnd[0] = T // 2
                tile(T - 1, 0)

        @block.scalar
        def _(act):
            act.wait_ge(s_const, 2)
            for layer in range(2):
                act.wait_ge(s_deg, layer + 1)
                nv = layer + 1

                def tile(t, first=False):
                    g = layer * T + t
                    if not first:
                        act.wait_ge(s_tr, g)
                    nc.scalar.activation(mean_nb, acc[:, ds(t, 1), 0:D].rearrange("p o d -> p (o d)"), ACT.Copy,
                                         scale=rdeg[:, ds(t, 1)]).then_inc(s_mean, 1)
                    act.wait_ge(s_tr, g + 1)
                    if not first:
                        act.wait_ge(s_proj, g)
                    nc.scalar.activation(t_nb, ps[:, 0, :], ACT.Copy)
                    nc.scalar.activation(t_own, ps[:, 1, :], ACT.Copy).then_inc(s_tc, 1)
                    for n in range(nv):
                        act.wait_ge(s_var, layer * T + nv * t + n + 1)
                        if not (first and n == 0):
                            pass
                        nc.scalar.activation(sd[:], mv[:, 1:2], ACT.Sqrt, bias=eps[:]).then_inc(s_sd, 1)
                tile(0, first=(layer == 0))
                with act.Fori(1, T) as t:
                    tile(t)


def kernel(x, src, dst, L0_gnn_W_l, L0_gnn_b_l, L0_gnn_W_r, L1_gnn_W_self, L1_gnn_b_self, L1_gnn_W_neigh,
           L1_gnn_b_neigh, L1_gnn_ln_gamma, L1_gnn_ln_beta):
    import numpy as np
    import concourse.bacc as bacc
    from concourse.bass_utils import run_bass_kernel_spmd

    nc = bacc.Bacc("TRN2", target_bir_lowering=False, num_devices=1)
    given = [("x", x), ("src", src), ("dst", dst), ("w_l_t", np.asarray(L0_gnn_W_l).T), ("b_l", L0_gnn_b_l),
             ("w_r_t", np.asarray(L0_gnn_W_r).T), ("w_self_t", np.asarray(L1_gnn_W_self).T),
             ("b_self", L1_gnn_b_self), ("w_neigh_t", np.asarray(L1_gnn_W_neigh).T), ("b_neigh", L1_gnn_b_neigh),
             ("gamma", L1_gnn_ln_gamma), ("beta", L1_gnn_ln_beta)]
    arrays, args = {}, []
    for name, a in given:
        a = np.ascontiguousarray(a)
        arrays[f"in_{name}"] = a
        args.append(nc.dram_tensor(f"in_{name}", a.shape, mybir.dt.from_np(a.dtype), kind="ExternalInput").ap())
    out = nc.dram_tensor("out_0", arrays["in_x"].shape, mybir.dt.float32, kind="ExternalOutput").ap()
    gnn_two_layers(nc, *args, out)
    r = run_bass_kernel_spmd(nc, [arrays], core_ids=[0])
    return r.results[0]["out_0"]
```

```python
import concourse.bass as bass
from concourse import mybir
from contextlib import ExitStack

P = 128


def gnn_two_layers(nc, x, src, dst, w_l_t, b_l, w_r_t, w_self_t, b_self, w_neigh_t, b_neigh, gamma, beta, out):
    f32, f16, bf16, i32 = mybir.dt.float32, mybir.dt.float16, mybir.dt.bfloat16, mybir.dt.int32
    ALU, ACT, AX = mybir.AluOpType, mybir.ActivationFunctionType, mybir.AxisListType
    ds = bass.ds

    N, D = x.shape
    E = src.shape[0]
    T = -(-N // P)
    LAST = N - (T - 1) * P
    KC = D // P
    U = 16
    H = U // 2
    EC = -(-(-(-E // P)) // U) * U
    EFULL, EREST = E // EC, E - E // EC * EC
    GROUP = (2, 2)
    GROUPS = [-(-(-(-E // (P * g)) + T - 1) * g // U) * U // g for g in GROUP]
    assert all((E + T * (P * g - 1)) // (P * g) <= n for n, g in zip(GROUPS, GROUP))
    CHUNKS = [n * g for n, g in zip(GROUPS, GROUP)]
    WIN = P * GROUP[0]
    NWIN = -(-E // WIN)
    WB = 4
    WP = NWIN // WB
    WREST = E - (NWIN - 1) * WIN
    assert WB * WP == NWIN and GROUPS[0] <= 512 and NWIN + T - 1 <= GROUPS[0]
    CW = max(CHUNKS)
    EPS = 1e-5
    GB = 8
    SB = 8
    PB = 4
    TW = 2 * D + 4
    XS = 14
    HS = 10
    assert D ** 0.5 * 2 ** HS < 65504
    BATCH = 7
    NOWHERE = 8191
    assert NOWHERE // P >= T
    assert T % BATCH == 0 and BATCH <= GB

    ctx = ExitStack()
    with ctx:
        def sb(name, shape, dt):
            return ctx.enter_context(nc.sbuf_tensor(name, shape, dt))

        def sem(name):
            return ctx.enter_context(nc.semaphore(name))

        tri = sb("tri", [P, P], f32)
        ones = sb("ones", [P, P], f32)
        ident = sb("ident", [P, P], f32)
        iota_node = sb("iota_node", [P, P], f16)
        iota_chunk = sb("iota_chunk", [P, CW], f16)
        iota_bin = sb("iota_bin", [P, T], f32)
        eps = sb("eps", [P, 1], f32)
        zeros = sb("zeros", [P, D + 1], f32)
        edges = sb("edges", [P, 2, EC], i32)
        flat = sb("flat", [P, 6 * EC], f32)
        inta, intb = (flat[:, k * EC:(k + 1) * EC].bitcast(i32) for k in (0, 1))
        val1, val2, run, pos = (flat[:, k * EC:(k + 1) * EC] for k in (2, 3, 4, 5))
        hi, lo = run, pos
        W4 = "p (b j) -> p b j"
        win_i = [flat[0:WP, k * WB * WIN:(k + 1) * WB * WIN].rearrange(W4, b=WB).bitcast(i32) for k in (0, 1)]
        win_f = [flat[0:WP, k * WB * WIN:(k + 1) * WB * WIN].rearrange(W4, b=WB) for k in (2, 3)]
        win_t = flat[0:WP, 4 * WB * WIN:4 * WB * WIN + WB * P].rearrange(W4, b=WB)
        binf = sb("binf", [P, EC], f16)
        mask = sb("mask", [P, EC], f16)
        totals = sb("totals", [P, T], f32)
        nch = sb("nch", [P, T], f32)
        nchi = sb("nchi", [P, T], i32)
        cend = sb("cend", [P, T], f32)
        cstart = sb("cstart", [P, T], f32)
        base = sb("base", [P, T], f32)
        cs_col = sb("cs_col", [T, 1], f32)
        past_bins = sb("past_bins", [T, 1], f32)
        w_ti = sb("w_ti", [WP, 2, WB], i32)
        w_tf = sb("w_tf", [WP, 2, WB], f32)
        w_n = sb("w_n", [WP, WB], f32)
        w_0 = sb("w_0", [WP, WB], f32)
        w_1 = sb("w_1", [WP, WB], f32)
        w_d = sb("w_d", [WP, WB], f32)
        bad = sb("bad", [P, 1], f32)
        unsorted = sb("unsorted", [1, 1], i32)
        spot = sb("spot", [P, PB, P], f16)
        put1 = sb("put1", [P, PB, P], f16)
        put2 = sb("put2", [P, PB, P], f16)
        where = sb("where", [P, PB, CW], f16)
        w_hot = where[0:WP, :, :].bitcast(f32).rearrange("p a c -> p (a c)")[:, 0:WB * GROUPS[0]].rearrange(
            "p (b c) -> p b c", b=WB)
        past = where[0:T, :, :].bitcast(f32).rearrange("p a c -> p (a c)")[:, 0:CW]
        g_idx = [sb(f"g_idx{l}", [P, CHUNKS[l]], i32) for l in range(2)]
        g_loc = [sb(f"g_loc{l}", [P, CHUNKS[l]], f32) for l in range(2)]
        g_tile = [sb(f"g_tile{l}", [1, CHUNKS[0]], i32) for l in range(2)]
        dst_next = g_idx[1][:, 0:EC]
        idx_ring = sb("idx_ring", [P, U], i32)
        loc_ring = sb("loc_ring", [P, U], f32)
        lo_ring = sb("lo_ring", [P, U], f32)
        hi_ring = sb("hi_ring", [P, U], f32)
        rows = sb("rows", [P, GB, TW], f16)
        onehot = sb("onehot", [P, SB, P], bf16)
        acc = sb("acc", [P, T, D + 1], f32)
        rdeg = sb("rdeg", [P, T], f32)
        has = sb("has", [P, T], f32)
        top = sb("top", [P, T], f32)
        scale = sb("scale", [P, T], f32)
        inv = sb("inv", [P, T], f32)
        w_a = sb("w_a", [P, KC, D], f32)
        w_b = sb("w_b", [P, KC, D], f32)
        vec = [where[:, :, :].bitcast(f32).rearrange("p a c -> p (a c)")[:, k * D:(k + 1) * D] for k in range(3)]
        vec += [edges[:, :, :].bitcast(f32).rearrange("p a c -> p (a c)")[:, k * D:(k + 1) * D] for k in range(2)]
        OB = 4
        plain = rows[:, :, :].rearrange("p b w -> p (b w)")
        own = plain[:, 0:2 * OB * D].bitcast(f32).rearrange("p (b d) -> p b d", b=OB)
        res = plain[:, 2 * OB * D:2 * (OB + 2) * D].bitcast(f32).rearrange("p (b d) -> p b d", b=2)
        assert 2 * (OB + 2) * D <= 6 * TW
        res_tab = rows[:, 6:8, :]
        mean_nb = flat[:, 0:2 * D].rearrange("p (b d) -> p b d", b=2)
        t_nb = flat[:, 2 * D:4 * D].rearrange("p (b d) -> p b d", b=2)
        t_own = flat[:, 4 * D:6 * D].rearrange("p (b d) -> p b d", b=2)
        r, y = flat[:, 6 * D:7 * D], flat[:, 7 * D:8 * D]
        st = sb("st", [P, 6], f32)
        mv = sb("mv", [P, 2], f32)
        sd = sb("sd", [P, 1], f32)
        rs = sb("rs", [P, 1], f32)
        ps = ctx.enter_context(nc.psum_tensor("ps", [P, 8, 512], f32))

        tables = [nc.dram_tensor(f"table{l}", [T * P, TW], f16, kind="Internal").ap() for l in range(2)]
        h_dram = nc.dram_tensor("h_scratch", [T * P, D], f32, kind="Internal").ap()

        s_pad = sem("s_pad")
        s_edges = sem("s_edges")
        s_wins = sem("s_wins")
        s_vec = sem("s_vec")
        s_x = [sem(f"s_x{k}") for k in range(5)]
        s_iota = sem("s_iota")
        s_sel = sem("s_sel")
        s_const = sem("s_const")
        s_w = sem("s_w")
        v = sem("v")
        s_scale = sem("s_scale")
        s_high = sem("s_high")
        s_low = sem("s_low")
        s_tail = sem("s_tail")
        s_tab = [sem(f"s_tab{k}") for k in range(BATCH)]
        s_zero = sem("s_zero")
        s_wn = sem("s_wn")
        s_w0 = sem("s_w0")
        s_whot = sem("s_whot")
        s_win = sem("s_win")
        s_flag = sem("s_flag")
        v_gen = sem("v_gen")
        lists = {0: {}, 1: {}}
        for l in range(2):
            for name in ("tot", "cnt", "cs", "cscol", "cscp", "past", "tile", "spot", "where", "put", "placed", "list"):
                lists[l][name] = sem(f"s_{name}{l}")
        s_idx = sem("s_idx")
        s_ring = sem("s_ring")
        s_row = [sem(f"s_row{k}") for k in range(GB)]
        s_hot = sem("s_hot")
        s_mm = sem("s_mm")
        s_acc = sem("s_acc")
        s_deg = sem("s_deg")
        s_own = [sem(f"s_own{k}") for k in range(OB)]
        s_mean = sem("s_mean")
        s_tr = sem("s_tr")
        s_tc = sem("s_tc")
        s_proj = sem("s_proj")
        s_var = sem("s_var")
        s_sd = sem("s_sd")
        s_res = sem("s_res")
        s_st = [sem(f"s_st{k}") for k in range(2)]

        block = ctx.enter_context(nc.Block())
        XG = 12

        def chunk0(layer):
            return layer * CHUNKS[0]

        def group0(layer):
            return layer * GROUPS[0]

        def slot_tiles(slots, k):
            return (T - 1 - k) // slots + 1

        def stored(layer, t, k):
            n = (t - k) // 2 + 1
            return 32 * n if layer == 0 else 32 * slot_tiles(2, k) + 16 * n

        def loaded(layer, t, k):
            return 16 * (layer * slot_tiles(OB, k) + (t - k) // OB + 1)

        def over_tiles(eng, body):
            for t in range(OB):
                body(t, t)
            with eng.Fori(1, T // OB - 1) as i:
                for k in range(OB):
                    body(OB * i + k, k)
            for t in range(T // OB * OB - OB, T):
                body(t, t % OB)

        @block.sync
        def _(sp):
            sp.wait_ge(s_pad, 3)
            for a, given in enumerate((src, dst)):
                sp.dma_start(edges[0:EFULL, a, :], given[0:EFULL * EC].rearrange("(p c) -> p c", c=EC)).then_inc(s_edges, 16)
                sp.dma_start(edges[EFULL:EFULL + 1, a, 0:EREST],
                             given[EFULL * EC:E].rearrange("(p c) -> p c", p=1)).then_inc(s_edges, 16)
            sp.dma_start(dst_next[0:EFULL, :], dst[1:EFULL * EC + 1].rearrange("(p c) -> p c", c=EC)).then_inc(s_edges, 16)
            sp.dma_start(dst_next[EFULL:EFULL + 1, 0:EREST - 1],
                         dst[EFULL * EC + 1:E].rearrange("(p c) -> p c", p=1)).then_inc(s_edges, 16)
            for a, given in enumerate((src, dst)):
                n = WP * WIN
                for b in range(WB - 1):
                    sp.dma_start(win_i[a][:, b, :], given[b * n:(b + 1) * n].rearrange("(p j) -> p j", j=WIN)).then_inc(s_wins, 16)
                sp.dma_start(win_i[a][0:WP - 1, WB - 1, :],
                             given[(WB - 1) * n:(NWIN - 1) * WIN].rearrange("(p j) -> p j", j=WIN)).then_inc(s_wins, 16)
                sp.dma_start(win_i[a][WP - 1:WP, WB - 1, 0:WREST],
                             given[(NWIN - 1) * WIN:E].rearrange("(p j) -> p j", p=1)).then_inc(s_wins, 16)
            for k in range(4):
                sp.dma_start(acc[:, k * XG:(k + 1) * XG, 0:D],
                             x[k * XG * P:(k + 1) * XG * P, :].rearrange("(t p) d -> p t d", p=P)).then_inc(s_x[k], 16)
            sp.dma_start(acc[0:LAST, T - 1, 0:D], x[(T - 1) * P:N, :]).then_inc(s_x[4], 16)
            with sp.Fori(0, T // BATCH) as i:
                for k in range(BATCH):
                    sp.wait_ge(s_high, BATCH * i + k + 1)
                    sp.wait_ge(s_low, BATCH * i + k + 1)
                    sp.wait_ge(s_tail, BATCH * i + k + 1)
                    sp.dma_start(tables[0][ds((BATCH * i + k) * P, P), :], rows[:, k, :]).then_inc(s_tab[k], 16)
            for layer in range(2):
                wa, wb = ((w_l_t, w_r_t), (w_neigh_t, w_self_t))[layer]
                if layer:
                    sp.wait_ge(s_proj, T)
                else:
                    sp.wait_ge(lists[1]["placed"], EC)
                    for n, a in enumerate((b_l, b_self, b_neigh, gamma, beta)):
                        sp.dma_start(vec[n], a.rearrange("(o d) -> o d", o=1).to_broadcast([P, D])).then_inc(s_vec, 16)
                sp.dma_start(w_a[:], wa.rearrange("(k p) n -> p k n", p=P)).then_inc(s_w, 16)
                sp.dma_start(w_b[:], wb.rearrange("(k p) n -> p k n", p=P)).then_inc(s_w, 16)
                source = (x, h_dram)[layer]
                target = (h_dram, out)[layer]

                def load(t, k, n=P):
                    sp.dma_start(own[0:n, k, :], source[ds(t * P, n), :] if not isinstance(t, int)
                                 else source[t * P:t * P + n, :]).then_inc(s_own[k], 16)

                def tile(t, k, load_next=True):
                    n = LAST if layer == 1 and isinstance(t, int) and t == T - 1 else P
                    sp.wait_ge(s_res, layer * T + t + 1)
                    rows_of = (lambda a: a[t * P:t * P + n, :]) if isinstance(t, int) else (lambda a: a[ds(t * P, n), :])
                    sp.dma_start(rows_of(target), res[0:n, k % 2, :]).then_inc(s_st[k % 2], 16)
                    if layer == 0:
                        sp.dma_start(rows_of(tables[1]), res_tab[0:n, k % 2, :]).then_inc(s_st[k % 2], 16)
                    if not isinstance(t, int) or t + OB < T:
                        last = isinstance(t, int) and t + OB == T - 1
                        load(t + OB, k, LAST if last and layer == 0 else P)

                sp.wait_ge(s_mm, chunk0(layer) + CHUNKS[layer])
                for t in range(OB):
                    load(t, t)
                over_tiles(sp, tile)
            for k in range(2):
                sp.wait_ge(s_st[k], stored(1, T - 1 - (T - 1 - k) % 2, k))

        @block.gpsimd
        def _(pool):
            nc.gpsimd.iota(iota_node[:], pattern=[[1, P]], base=0, channel_multiplier=0,
                           allow_small_or_imprecise_dtypes=True).then_inc(s_iota, 1)
            nc.gpsimd.iota(iota_chunk[:], pattern=[[1, CW]], base=0, channel_multiplier=0,
                           allow_small_or_imprecise_dtypes=True).then_inc(s_iota, 1)
            nc.gpsimd.iota(iota_bin[:], pattern=[[1, T]], base=0, channel_multiplier=0,
                           allow_small_or_imprecise_dtypes=True).then_inc(s_iota, 1)
            nc.gpsimd.memset(tri[:], 1.0).then_inc(s_sel, 1)
            nc.gpsimd.memset(ident[:], 0.0).then_inc(s_sel, 1)
            nc.gpsimd.memset(ones[:], 1.0).then_inc(s_const, 1)
            nc.gpsimd.memset(zeros[:], 0.0)
            nc.gpsimd.memset(eps[:], EPS).then_inc(s_const, 1)
            pool.wait_ge(s_sel, 2)
            nc.gpsimd.affine_select(out=tri[:], in_=tri[:], compare_op=ALU.is_gt, fill=0.0, base=0,
                                    pattern=[[1, P]], channel_multiplier=-1).then_inc(s_const, 1)
            nc.gpsimd.affine_select(out=ident[:], in_=ident[:], compare_op=ALU.not_equal, fill=1.0, base=0,
                                    pattern=[[1, P]], channel_multiplier=-1).then_inc(s_const, 1)
            pool.wait_ge(s_scale, 1)
            with pool.Fori(0, T // BATCH) as i:
                for k in range(BATCH):
                    pool.wait_ge(s_high, BATCH * i + k + 1)
                    nc.gpsimd.tensor_copy(rows[:, k, 2 * D:2 * D + 2].bitcast(f32), scale[:, ds(BATCH * i + k, 1)])
                    nc.gpsimd.tensor_copy(rows[:, k, 2 * D + 2:2 * D + 4].bitcast(bf16)[:, 0:1],
                                          inv[:, ds(BATCH * i + k, 1)])
                    nc.gpsimd.tensor_copy(rows[:, k, 2 * D + 2:2 * D + 4].bitcast(bf16)[:, 1:2],
                                          inv[:, ds(BATCH * i + k, 1)]).then_inc(s_tail, 1)
            for k in range(7):
                pool.wait_ge(s_low, (k + 1) * T // 7)
                nc.gpsimd.memset(acc[:, k * T // 7:(k + 1) * T // 7, :], 0.0).then_inc(s_zero, 1)

            for layer in range(2):
                if layer == 0:
                    for k in range(BATCH):
                        pool.wait_ge(s_tab[k], 16 * (T // BATCH))
                else:
                    def clear(t, k):
                        pool.wait_ge(s_mean, t + 1)
                        nc.gpsimd.tensor_copy(acc[:, ds(t, 1), :].rearrange("p o d -> p (o d)"),
                                              zeros[:]).then_inc(s_zero, 1)
                    over_tiles(pool, clear)
                    for k in range(2):
                        pool.wait_ge(s_st[k], stored(0, T - 1 - (T - 1 - k) % 2, k))

                def gathers(i, first=False):
                    for k in range(U):
                        if k % H == 0:
                            pool.wait_ge(s_idx, (layer * CHUNKS[0]) // H + 2 * i + k // H + 1)
                        if not (first and k < GB):
                            used = chunk0(layer) + U * i + k - GB + 1
                            if not isinstance(used, int):
                                used = pool.to_reg(used)
                            pool.wait_ge(s_sel, 2)
                            pool.wait_ge(s_mm, used)
                        nc.gpsimd.indirect_dma_start(
                            out=rows[:, k % GB, :], out_offset=None, in_=tables[layer][:, :],
                            in_offset=bass.IndirectOffsetOnAxis(ap=idx_ring[:, k:k + 1], axis=0),
                        ).then_inc(s_row[k % GB], 16)

                gathers(0, first=(layer == 0))
                with pool.Fori(1, CHUNKS[layer] // U) as i:
                    gathers(i)

        @block.vector
        def _(dve):
            V = nc.vector
            steps = [0]
            chain = [v]

            def link(ins):
                steps[0] += 1
                ins.then_inc(chain[0], 1)
                dve.wait_ge(chain[0], steps[0])

            def loop(n, per, body, start=0):
                begun = steps[0]
                with dve.Fori(start, n) as i:
                    steps[0] = begun + (i - start) * per
                    body(i)
                steps[0] = begun + (n - start) * per

            V.memset(edges[:], NOWHERE).then_inc(s_pad, 1)
            V.memset(dst_next, 1 << 20).then_inc(s_pad, 1)
            V.memset(acc[:, T - 1, 0:D], 0.0)
            link(V.memset(past_bins[:], 1.0))
            V.memset(past_bins[0:1, :], 0.0)
            V.memset(win_i[0][:, WB - 1, :], 0)
            V.memset(win_i[1][:, WB - 1, :], 1 << 20).then_inc(s_pad, 1)

            dve.wait_ge(s_edges, 16 * 6)
            link(V.tensor_tensor(pos[:, 0:EC], edges[:, 1, :], dst_next, ALU.is_gt))
            V.tensor_reduce(bad[:], pos[:, 0:EC], AX.X, ALU.add).then_inc(s_flag, 1)

            dve.wait_ge(s_wins, 16 * 2 * (WB + 1))
            dve.wait_ge(s_iota, 3)
            for a in range(2):
                V.tensor_copy(win_f[a], win_i[a])
            link(V.tensor_scalar(w_ti[:, 0, :], win_i[1][:, :, 0], 7, None, ALU.arith_shift_right))
            link(V.tensor_scalar(w_ti[:, 1, :], win_i[1][:, :, WIN - 1], 7, None, ALU.arith_shift_right))
            link(V.tensor_scalar(w_tf[:], w_ti[:], float(T - 1), None, ALU.min))
            V.scalar_tensor_tensor(w_n[:], w_tf[:, 1, :], 1.0, w_tf[:, 0, :], ALU.add, ALU.subtract).then_inc(s_wn, 1)
            dve.wait_ge(s_w0, 1)
            link(V.tensor_copy(w_0[:], ps[0:WP, 0, 0:WB]))
            link(V.tensor_tensor(w_1[:], w_0[:], w_n[:], ALU.add))
            link(V.tensor_tensor(w_d[:], w_tf[:, 0, :], w_0[:], ALU.subtract))
            for b in range(WB):
                V.tensor_scalar(win_t[:, b, :], ones[0:WP, :], w_d[:, b:b + 1], None, ALU.mult)
                link(V.tensor_scalar(w_hot[:, b, :], iota_chunk[0:WP, 0:GROUPS[0]], w_0[:, b:b + 1], None, ALU.is_ge))
                V.scalar_tensor_tensor(w_hot[:, b, :], iota_chunk[0:WP, 0:GROUPS[0]], w_1[:, b:b + 1],
                                       w_hot[:, b, :], ALU.is_lt, ALU.mult).then_inc(s_whot, 1)
            dve.wait_ge(s_flag, 2)
            V.tensor_scalar(unsorted[:], ps[0:1, 0, 64:65], 1.0, None, ALU.min).then_inc(s_flag, 1)
            for k in range(5):
                tiles = slice(k * XG, min((k + 1) * XG, T))
                dve.wait_ge(s_x[k], 16)
                link(V.tensor_reduce(top[:, tiles], acc[:, tiles, 0:D], AX.X, ALU.max, apply_absolute_value=True))
            link(V.tensor_scalar(top[:], top[:], 2.0 ** -60, None, ALU.max))
            link(V.tensor_scalar(top[:].bitcast(i32), top[:].bitcast(i32), 0x7F800000, None, ALU.bitwise_and))
            link(V.tensor_scalar(scale[:], top[:], 2.0 ** -XS, None, ALU.mult))
            V.reciprocal(inv[:], scale[:]).then_inc(s_scale, 1)

            group = "p (c g) -> p c g"
            dve.wait_ge(s_win, 1)
            tile_of = pos[:, 0:GROUPS[0]]
            link(V.tensor_tensor(tile_of, ps[:, 1, 0:GROUPS[0]], iota_chunk[:, 0:GROUPS[0]], ALU.add))
            link(V.tensor_scalar(tile_of, tile_of, float(T - 1), 0.0, ALU.min, ALU.max))
            link(V.tensor_copy(g_tile[0][:, 0:GROUPS[0]], tile_of[0:1, :]))
            for s in range(2):
                link(V.tensor_copy(g_idx[0][:].rearrange(group, g=2)[:, :, s], ps[:, 2 + s, 0:GROUPS[0]]))
                link(V.scalar_tensor_tensor(g_loc[0][:].rearrange(group, g=2)[:, :, s], tile_of, -float(P),
                                            ps[:, 4 + s, 0:GROUPS[0]], ALU.mult, ALU.add))

            dve.wait_ge(s_scale, 1)

            def low(i, first=False):
                for k in range(BATCH):
                    dve.wait_ge(s_high, BATCH * i + k + 1)
                    V.scalar_tensor_tensor(rows[:, k, D:2 * D],
                                           acc[:, ds(BATCH * i + k, 1), 0:D].rearrange("p o d -> p (o d)"),
                                           inv[:, ds(BATCH * i + k, 1)], rows[:, k, 0:D], ALU.mult,
                                           ALU.subtract).then_inc(s_low, 1)
            with dve.Fori(0, T // BATCH) as i:
                low(i)

            def prepare(layer):
                key, other, s = edges[:, 1 - layer, :], edges[:, layer, :], lists[layer]
                g = GROUP[layer]
                link(V.tensor_scalar(inta, key, 7, None, ALU.arith_shift_right))
                link(V.tensor_copy(binf[:], inta))
                link(V.tensor_scalar(inta, other, 3, None, ALU.arith_shift_right))
                link(V.tensor_copy(val1, inta))
                link(V.tensor_scalar(inta, other, 7, 8, ALU.bitwise_and, ALU.logical_shift_left))
                link(V.tensor_scalar(intb, key, 127, None, ALU.bitwise_and))
                link(V.scalar_tensor_tensor(val2, inta, 1.0, intb, ALU.add, ALU.add))

                def count(b):
                    link(V.tensor_scalar(mask[:], binf[:], iota_bin[:, ds(b, 1)], 0.0, ALU.is_equal, ALU.add,
                                         accum_out=totals[:, ds(b, 1)]))
                loop(T, 1, count)
                V.memset(pos, -1.0).then_inc(s["tot"], 1)
                dve.wait_ge(s["cnt"], 1)
                link(V.tensor_scalar(nchi[:], ps[:, 0, 0:T], float(P * g - 1), None, ALU.add))
                link(V.tensor_scalar(nchi[:], nchi[:], 7 + g - 1, None, ALU.arith_shift_right))
                link(V.tensor_copy(nch[:], nchi[:]))
                link(V.tensor_tensor_scan(cend[:], nch[:], nch[:], 0.0, ALU.add, ALU.bypass))
                link(V.tensor_tensor(cstart[:], cend[:], nch[:], ALU.subtract))
                link(V.tensor_scalar(base[:], cstart[:], float(P * g), None, ALU.mult))
                V.tensor_tensor(base[:], base[:], ps[:, 0, 64:64 + T], ALU.add).then_inc(s["cs"], 1)
                dve.wait_ge(s["cs"], 1)
                dve.wait_ge(s["cscol"], 1)
                V.tensor_copy(cs_col[:], ps[0:T, 0, 128:129]).then_inc(s["cscp"], 1)
                dve.wait_ge(s["cscp"], 1)
                V.tensor_scalar(past, iota_chunk[0:T, :], cs_col[:, 0:1], None, ALU.is_ge).then_inc(s["past"], 1)
                dve.wait_ge(s["past"], 1)

                def place(b):
                    link(V.tensor_scalar(mask[:], binf[:], iota_bin[:, ds(b, 1)], None, ALU.is_equal))
                    link(V.tensor_tensor_scan(run, mask[:], mask[:], base[:, ds(b, 1)], ALU.add, ALU.bypass))
                    link(V.tensor_tensor(run, run, mask[:], ALU.mult))
                    link(V.tensor_tensor(pos, pos, run, ALU.add))
                loop(T, 4, place)
                link(V.tensor_copy(inta, pos))
                link(V.tensor_scalar(intb, inta, 7, None, ALU.arith_shift_right))
                link(V.tensor_copy(hi, intb))
                link(V.tensor_scalar(intb, inta, 127, None, ALU.bitwise_and))
                link(V.tensor_copy(lo, intb))
                dve.wait_ge(s["tile"], 1)
                n = GROUPS[layer]
                half = n // 2
                V.tensor_copy(g_tile[layer][:, 0:n].rearrange("p (h c) -> p h c", h=2),
                              ps[0:1, 0:2, 0:half]).then_inc(s["list"], 1)

            def unpack(layer):
                s, n = lists[layer], CHUNKS[layer]
                dve.wait_ge(s["placed"], EC)
                halves = "p (h c) -> p h c"
                v2i, v2h = (flat[:, k * 1024:k * 1024 + n].bitcast(i32) for k in (0, 1))
                link(V.tensor_copy(v2i.rearrange(halves, h=2), ps[:, 2:4, 0:n // 2]))
                link(V.tensor_scalar(v2h, v2i, 8, None, ALU.arith_shift_right))
                link(V.scalar_tensor_tensor(g_idx[layer][:].rearrange(halves, h=2), ps[:, 0:2, 0:n // 2], 8.0,
                                            v2h.rearrange(halves, h=2), ALU.mult, ALU.add))
                link(V.tensor_scalar(v2h, v2i, 255, None, ALU.bitwise_and))
                link(V.tensor_scalar(g_loc[layer][:], v2h, -1.0, None, ALU.add))

            dve.wait_ge(s_flag, 3)
            flag = dve.value_load(unsorted[0:1, 0:1], min_val=0, max_val=1)
            with dve.If(flag > 0):
                outer, steps[0], chain[0] = steps[0], 0, v_gen
                prepare(0)

                def bin_column(c, k, first=False):
                    s = lists[0]
                    col = PB * c + k
                    if not first:
                        dve.wait_ge(s["placed"], col - PB + 1)
                    V.tensor_scalar(put1[:, k, :], iota_node[:], lo[:, ds(col, 1)], val1[:, ds(col, 1)],
                                    ALU.is_equal, ALU.mult)
                    V.tensor_scalar(put2[:, k, :], iota_node[:], lo[:, ds(col, 1)], val2[:, ds(col, 1)],
                                    ALU.is_equal, ALU.mult)
                    V.tensor_scalar(where[:, k, 0:CHUNKS[0]], iota_chunk[:, 0:CHUNKS[0]], hi[:, ds(col, 1)], None,
                                    ALU.is_equal).then_inc(s["where"], 1)
                for k in range(PB):
                    bin_column(0, k, first=True)
                with dve.Fori(1, EC // PB) as c:
                    for k in range(PB):
                        bin_column(c, k)
                unpack(0)
                steps[0], chain[0] = outer, v

            prepare(1)

            def hand_over(layer, i, half):
                V.tensor_copy(loc_ring[:, half * H:half * H + H], g_loc[layer][:, ds(i * U + half * H, H)])
                V.tensor_copy(idx_ring[:, half * H:half * H + H],
                              g_idx[layer][:, ds(i * U + half * H, H)]).then_inc(s_idx, 1)

            def hot(layer, i, k, first):
                n = chunk0(layer) + U * i + k
                dve.wait_ge(s_row[k % GB], 16 * (chunk0(layer) // GB + (U // GB) * i + k // GB + 1))
                assert SB == GB
                V.tensor_scalar(onehot[:, k % SB, :], iota_node[:], loc_ring[:, k:k + 1],
                                rows[:, k % GB, 2 * D:2 * D + 2].bitcast(f32), ALU.is_equal, ALU.mult).then_inc(s_hot, 1)

            def add(layer, i, q, first=False):
                g = GROUP[layer]
                done = group0(layer) + U // g * i + q
                tile = dve.value_load(g_tile[layer][0:1, ds(U // g * i + q, 1)], min_val=0, max_val=T - 1)
                if not (first and q == 0):
                    dve.wait_ge(s_acc, done)
                dve.wait_ge(s_mm, chunk0(layer) + U * i + g * (q + 1))
                part = ps[:, 4 + 2 * (q % 2):6 + 2 * (q % 2), :].rearrange("p b c -> p (b c)")[:, 0:D + 1]
                tile_acc = acc[:, ds(tile, 1), :].rearrange("p o d -> p (o d)")
                V.tensor_tensor(tile_acc, tile_acc, part, ALU.add).then_inc(s_acc, 1)

            def spots(i, k, first):
                s, col = lists[1], U * i + k
                if k == 0:
                    if not first:
                        dve.wait_ge(s["where"], U * i)
                    V.tensor_copy(lo_ring[:], lo[:, ds(U * i, U)])
                    V.tensor_copy(hi_ring[:], hi[:, ds(U * i, U)]).then_inc(s_ring, 1)
                    dve.wait_ge(s_ring, i + 1)
                if not (first and k < PB):
                    dve.wait_ge(s["placed"], col - PB + 1)
                V.tensor_scalar(spot[:, k % PB, :], iota_node[:], lo_ring[:, k:k + 1], None,
                                ALU.is_equal).then_inc(s["spot"], 1)
                V.tensor_scalar(where[:, k % PB, 0:CHUNKS[1]], iota_chunk[:, 0:CHUNKS[1]], hi_ring[:, k:k + 1], None,
                                ALU.is_equal).then_inc(s["where"], 1)

            def chunks(layer, i, first=False, last=False, place=False):
                g = GROUP[layer]
                for k in range(U):
                    if k % H == 0 and not (first and layer == 0 and k == 0):
                        dve.wait_ge(s_hot, chunk0(layer) + U * i + k)
                    if k == 0:
                        hand_over(layer, i, 1)
                        dve.wait_ge(s_idx, (layer * CHUNKS[0]) // H + 2 * i + 1)
                    if k == H and not last:
                        hand_over(layer, i + 1, 0)
                        dve.wait_ge(s_idx, (layer * CHUNKS[0]) // H + 2 * i + 2)
                    if place:
                        spots(i, k, first)
                    hot(layer, i, k, first and layer == 0)
                    if k % g == 0 and k // g >= 2:
                        add(layer, i, k // g - 2, first and layer == 0)
                    elif k % g == 0 and not first:
                        add(layer, i - 1, U // g - 2 + k // g)
                if last:
                    add(layer, i, U // g - 2)
                    add(layer, i, U // g - 1)

            for layer in range(2):
                iters = CHUNKS[layer] // U
                if layer == 0:
                    hand_over(0, 0, 0)
                    dve.wait_ge(s_zero, 7)
                    chunks(0, 0, first=True, place=True)
                    with dve.Fori(1, EC // U) as i:
                        chunks(0, i, place=True)
                    with dve.Fori(EC // U, iters - 1) as i:
                        chunks(0, i)
                    chunks(0, iters - 1, last=True)
                    unpack(1)
                else:
                    dve.wait_ge(s_hot, CHUNKS[0])
                    hand_over(1, 0, 0)
                    dve.wait_ge(s_zero, 7 + T)
                    chunks(1, 0, first=True)
                    with dve.Fori(1, iters - 1) as i:
                        chunks(1, i)
                    chunks(1, iters - 1, last=True)
                dve.wait_ge(s_acc, group0(layer) + GROUPS[layer])
                link(V.tensor_scalar(rdeg[:], acc[:, :, D], 1.0, None, ALU.max))
                link(V.tensor_scalar(has[:], acc[:, :, D], 1.0, None, ALU.min))
                V.reciprocal(rdeg[:], rdeg[:]).then_inc(s_deg, 1)
                if layer == 0:
                    dve.wait_ge(s_vec, 16 * 5)
                    for k in range(2):
                        V.memset(res_tab[:, k, 2 * D:2 * D + 2].bitcast(f32), 2.0 ** -HS)
                        V.memset(res_tab[:, k, 2 * D + 2:2 * D + 4].bitcast(bf16), 2.0 ** HS)

                begun, per = steps[0], (6, 11)[layer]

                def norm_stats(dest, n):
                    V.bn_stats(st[:], dest).then_inc(v, 1)
                    steps[0] += 1
                    now = steps[0] if isinstance(steps[0], int) else dve.to_reg(steps[0])
                    dve.wait_ge(s_edges, 96)
                    dve.wait_ge(v, now)
                    V.bn_aggr(mv[:], st[:]).then_inc(s_var, 1)
                    dve.wait_ge(s_var, n + 1)
                    dve.wait_ge(s_sd, n + 1)
                    link(V.reciprocal(rs[:], sd[:]))

                def tile(t, k):
                    g = layer * T + t
                    steps[0] = begun + t * per
                    part, slot = ps[:, 4 + 2 * (k % 2), :], k % 2
                    dve.wait_ge(s_proj, g + 1)
                    if not (isinstance(t, int) and t < 2):
                        free = stored(layer, t - 2, slot)
                    else:
                        free = stored(0, T - 1 - (T - 1 - slot) % 2, slot) if layer else None
                    if layer == 0:
                        link(V.scalar_tensor_tensor(r, vec[0], has[:, ds(t, 1)], part, ALU.mult, ALU.add))
                        link(V.tensor_tensor(r, r, own[:, k, :], ALU.add))
                        norm_stats(r, t)
                        if free is not None:
                            dve.wait_ge(s_st[slot], free)
                        link(V.tensor_scalar(res[:, slot, :], r, mv[:, 0:1], rs[:, 0:1], ALU.subtract, ALU.mult))
                        link(V.tensor_scalar(res_tab[:, slot, 0:D], res[:, slot, :], 2.0 ** HS, None, ALU.mult))
                        V.scalar_tensor_tensor(res_tab[:, slot, D:2 * D], res[:, slot, :], 2.0 ** HS,
                                               res_tab[:, slot, 0:D], ALU.mult, ALU.subtract).then_inc(s_res, 1)
                    else:
                        link(V.scalar_tensor_tensor(r, vec[2], has[:, ds(t, 1)], part, ALU.mult, ALU.add))
                        link(V.tensor_tensor(r, r, vec[1], ALU.add))
                        link(V.scalar_tensor_tensor(r, r, 0.0, own[:, k, :], ALU.max, ALU.add))
                        norm_stats(r, T + 2 * t)
                        link(V.tensor_scalar(y, r, mv[:, 0:1], rs[:, 0:1], ALU.subtract, ALU.mult))
                        link(V.tensor_tensor(y, y, vec[3], ALU.mult))
                        link(V.tensor_tensor(y, y, vec[4], ALU.add))
                        link(V.tensor_tensor(y, y, own[:, k, :], ALU.add))
                        norm_stats(y, T + 2 * t + 1)
                        if free is not None:
                            dve.wait_ge(s_st[slot], free)
                        V.tensor_scalar(res[:, slot, :], y, mv[:, 0:1], rs[:, 0:1], ALU.subtract,
                                        ALU.mult).then_inc(s_res, 1)
                    if isinstance(t, int):
                        assert steps[0] == begun + (t + 1) * per, (steps[0], begun, t)

                over_tiles(dve, tile)

        @block.tensor
        def _(pe):
            def mm(*args, **kw):
                return nc.tensor.matmul(*args, skip_group_check=True, **kw)

            pe.wait_ge(s_const, 4)
            pe.wait_ge(s_flag, 1)
            mm(ps[:, 0, 64:65], ones[:], bad[:], start=True, stop=True).then_inc(s_flag, 1)
            pe.wait_ge(s_wn, 1)
            for b in range(WB):
                last = mm(ps[0:WP, 0, b:WB], (tri if b == 0 else ones)[0:WP, 0:WP], w_n[:, 0:WB - b],
                          start=(b == 0), stop=(b == WB - 1))
            last.then_inc(s_w0, 1)
            pe.wait_ge(s_whot, WB)
            for bank, lhs in ((1, win_t), (2, win_f[0]), (3, win_f[0]), (4, win_f[1]), (5, win_f[1])):
                at = bank % 2 * P if bank > 1 else 0
                for b in range(WB):
                    last = mm(ps[:, bank, 0:GROUPS[0]], lhs[:, b, at:at + P], w_hot[:, b, :],
                              start=(b == 0), stop=(b == WB - 1))
            last.then_inc(s_win, 1)

            def prepare(layer):
                s = lists[layer]
                pe.wait_ge(s["tot"], 1)
                mm(ps[:, 0, 0:T], ones[:], totals[:], start=True, stop=True)
                mm(ps[:, 0, 64:64 + T], tri[:], totals[:], start=True, stop=True).then_inc(s["cnt"], 1)
                pe.wait_ge(s["cs"], 1)
                mm(ps[0:T, 0, 128:129], cstart[0:1, :], ones[0:1, 0:1], start=True, stop=True).then_inc(s["cscol"], 1)
                pe.wait_ge(s["past"], 1)
                half = GROUPS[layer] // 2
                for b in range(2):
                    last = mm(ps[0:1, b, 0:half], past_bins[:, 0:1], past[:, b * half:(b + 1) * half],
                              start=True, stop=True)
                last.then_inc(s["tile"], 1)
                pe.wait_ge(s["list"], 1)

            def place(layer, col, k, start=False, stop=False):
                s, half = lists[layer], CHUNKS[layer] // 2
                pe.wait_ge(s["where"], col + 1)
                if layer:
                    pe.wait_ge(s["put"], col + 1)
                for n, put in enumerate((put1, put2)):
                    for b in range(2):
                        last = mm(ps[:, 2 * n + b, 0:half], put[:, k % PB, :],
                                  where[:, k % PB, b * half:(b + 1) * half], start=start, stop=stop)
                last.then_inc(s["placed"], 1)

            pe.wait_ge(s_flag, 3)
            flag = pe.value_load(unsorted[0:1, 0:1], min_val=0, max_val=1)
            with pe.If(flag > 0):
                prepare(0)
                for k in range(PB):
                    place(0, k, k, start=(k == 0))
                with pe.Fori(1, EC // PB - 1) as c:
                    for k in range(PB):
                        place(0, PB * c + k, k)
                for k in range(PB):
                    place(0, EC - PB + k, k, stop=(k == PB - 1))
            prepare(1)

            def sums(layer, i, first=False, placing=None):
                g = GROUP[layer]
                for k in range(U):
                    if placing is not None:
                        place(1, U * i + k, k, start=(placing == "first" and k == 0),
                              stop=(placing == "last" and k == U - 1))
                    q = k // g
                    bank = 4 + 2 * (q % 2)
                    n = chunk0(layer) + U * i + k
                    pe.wait_ge(s_hot, n + 1)
                    if k % g == 0 and not (first and q < 2):
                        pe.wait_ge(s_acc, group0(layer) + U // g * i + q - 1)
                    start, stop = k % g == 0, k % g == g - 1
                    lhs, row = onehot[:, k % SB, :], rows[:, k % GB, :]
                    mm(ps[:, bank, :], lhs, row[:, 0:D], start=start, stop=False)
                    mm(ps[:, bank, :], lhs, row[:, D:2 * D], start=False, stop=stop)
                    mm(ps[:, bank + 1, 0:1], lhs, row[:, 2 * D + 2:2 * D + 4].bitcast(bf16)[:, 0:1],
                       start=start, stop=stop).then_inc(s_mm, 1)

            for layer in range(2):
                iters = CHUNKS[layer] // U
                if layer == 0:
                    sums(0, 0, first=True, placing="first")
                    with pe.Fori(1, EC // U - 1) as i:
                        sums(0, i, placing="middle")
                    sums(0, EC // U - 1, placing="last")
                    with pe.Fori(EC // U, iters) as i:
                        sums(0, i)
                else:
                    with pe.Fori(0, iters) as i:
                        sums(1, i)
                pe.wait_ge(s_acc, group0(layer) + GROUPS[layer])
                pe.wait_ge(s_w, 32 * (layer + 1))

                def turn(t, k):
                    g = layer * T + t
                    pe.wait_ge(s_mean, g + 1)
                    if not (isinstance(g, int) and g == 0):
                        pe.wait_ge(s_tc, g)
                    for j in range(KC):
                        nc.tensor.transpose(ps[:, 0, j * P:(j + 1) * P], mean_nb[:, k % 2, j * P:(j + 1) * P], ident[:])
                    pe.wait_ge(s_own[k % OB], loaded(layer, t, k % OB))
                    for j in range(KC):
                        last = nc.tensor.transpose(ps[:, 1, j * P:(j + 1) * P], own[:, k % OB, j * P:(j + 1) * P], ident[:])
                    last.then_inc(s_tr, 1)

                def tile(t, k):
                    g = layer * T + t
                    if not (isinstance(t, int) and t == T - 1):
                        turn(t + 1, k + 1)
                    pe.wait_ge(s_tc, g + 1)
                    if not (isinstance(g, int) and g < 2):
                        pe.wait_ge(s_res, g - 1)
                    for n, (lhs, w) in enumerate(((t_nb, w_a), (t_own, w_b))):
                        for j in range(KC):
                            last = mm(ps[:, 4 + 2 * (k % 2), :], lhs[:, k % 2, j * P:(j + 1) * P], w[:, j, :],
                                      start=(n == 0 and j == 0), stop=(n == 1 and j == KC - 1))
                    last.then_inc(s_proj, 1)

                turn(0, 0)
                over_tiles(pe, tile)

        @block.scalar
        def _(act):
            act.wait_ge(s_const, 2)
            act.wait_ge(s_scale, 1)

            def high(i, first=False):
                for k in range(BATCH):
                    if not first:
                        act.wait_ge(s_tab[k], 16 * i)
                    nc.scalar.activation(rows[:, k, 0:D], acc[:, ds(BATCH * i + k, 1), 0:D].rearrange("p o d -> p (o d)"),
                                         ACT.Copy, scale=inv[:, ds(BATCH * i + k, 1)]).then_inc(s_high, 1)
            high(0, first=True)
            with act.Fori(1, T // BATCH) as i:
                high(i)

            def puts(c, first=False):
                s = lists[1]
                for k in range(PB):
                    col = PB * c + k
                    act.wait_ge(s["spot"], col + 1)
                    if not first:
                        act.wait_ge(s["placed"], col - PB + 1)
                    nc.scalar.activation(put1[:, k, :], spot[:, k, :], ACT.Copy, scale=val1[:, ds(col, 1)])
                    nc.scalar.activation(put2[:, k, :], spot[:, k, :], ACT.Copy,
                                         scale=val2[:, ds(col, 1)]).then_inc(s["put"], 1)
            puts(0, first=True)
            with act.Fori(1, EC // PB) as c:
                puts(c)

            for layer in range(2):
                act.wait_ge(s_deg, layer + 1)

                def mean(t, k):
                    g = layer * T + t
                    if not (isinstance(g, int) and g < 2):
                        act.wait_ge(s_tr, g - 1)
                    nc.scalar.activation(mean_nb[:, k % 2, :], acc[:, ds(t, 1), 0:D].rearrange("p o d -> p (o d)"),
                                         ACT.Copy, scale=rdeg[:, ds(t, 1)]).then_inc(s_mean, 1)

                def turned(t, k):
                    g = layer * T + t
                    act.wait_ge(s_tr, g + 1)
                    if not (isinstance(g, int) and g < 2):
                        act.wait_ge(s_proj, g - 1)
                    nc.scalar.activation(t_nb[:, k % 2, :], ps[:, 0, :], ACT.Copy)
                    nc.scalar.activation(t_own[:, k % 2, :], ps[:, 1, :], ACT.Copy).then_inc(s_tc, 1)

                def tile(t, k):
                    if not (isinstance(t, int) and t + 2 >= T):
                        mean(t + 2, k)
                    if not (isinstance(t, int) and t + 1 >= T):
                        turned(t + 1, k + 1)
                    nv = layer + 1
                    for n in range(nv):
                        act.wait_ge(s_var, layer * T + nv * t + n + 1)
                        nc.scalar.activation(sd[:], mv[:, 1:2], ACT.Sqrt, bias=eps[:]).then_inc(s_sd, 1)

                mean(0, 0)
                mean(1, 1)
                turned(0, 0)
                over_tiles(act, tile)


def kernel(x, src, dst, L0_gnn_W_l, L0_gnn_b_l, L0_gnn_W_r, L1_gnn_W_self, L1_gnn_b_self, L1_gnn_W_neigh,
           L1_gnn_b_neigh, L1_gnn_ln_gamma, L1_gnn_ln_beta):
    import numpy as np
    import concourse.bacc as bacc
    from concourse.bass_utils import run_bass_kernel_spmd

    nc = bacc.Bacc("TRN2", target_bir_lowering=False, num_devices=1)
    given = [("x", x), ("src", src), ("dst", dst), ("w_l_t", np.asarray(L0_gnn_W_l).T), ("b_l", L0_gnn_b_l),
             ("w_r_t", np.asarray(L0_gnn_W_r).T), ("w_self_t", np.asarray(L1_gnn_W_self).T),
             ("b_self", L1_gnn_b_self), ("w_neigh_t", np.asarray(L1_gnn_W_neigh).T), ("b_neigh", L1_gnn_b_neigh),
             ("gamma", L1_gnn_ln_gamma), ("beta", L1_gnn_ln_beta)]
    arrays, args = {}, []
    for name, a in given:
        a = np.ascontiguousarray(a)
        arrays[f"in_{name}"] = a
        args.append(nc.dram_tensor(f"in_{name}", a.shape, mybir.dt.from_np(a.dtype), kind="ExternalInput").ap())
    out = nc.dram_tensor("out_0", arrays["in_x"].shape, mybir.dt.float32, kind="ExternalOutput").ap()
    gnn_two_layers(nc, *args, out)
    r = run_bass_kernel_spmd(nc, [arrays], core_ids=[0])
    return r.results[0]["out_0"]
```
